# Optimizing a Trainium2 kernel written in Bass

```python
import numpy as np
import jax
import jax.numpy as jnp

def _softmax(x, axis=-1):
    return jax.nn.softmax(x, axis=axis)

def _gelu(x):
    return jax.nn.gelu(x, approximate=True)

def _silu(x):
    return jax.nn.silu(x)

def _sigmoid(x):
    return jax.nn.sigmoid(x)

def _layernorm(x, axis=-1, eps=1e-05):
    m = jnp.mean(x, axis=axis, keepdims=True)
    v = jnp.var(x, axis=axis, keepdims=True)
    return (x - m) / jnp.sqrt(v + eps)

def _scatter_add(tgt, idx, src, axis=0):
    return tgt.at[idx].add(src)

def _segment_sum(src, seg, n):
    return jax.ops.segment_sum(src, seg, n)
kernel_name = 'mk_gnn_preln_d4_gnn_r32_960b0e'

def setup_inputs(seed: int=0):
    np.random.seed(seed)
    _w = jnp.asarray

    def _rec_inputs():
        import jax
        import jax.numpy as jnp
        _gk = jax.random.key(seed)
        x = -0.0005121 + 1.001 * jax.random.normal(jax.random.fold_in(_gk, 1), (3125, 64), jnp.float32)
        src = jax.random.randint(jax.random.fold_in(_gk, 2), (50000,), 0, 3125, jnp.int32)
        dst = jnp.minimum((3125 * jax.random.uniform(jax.random.fold_in(_gk, 3), (50000,)) ** 2.0).astype(jnp.int32), 99999)
        _o = jnp.argsort(dst, stable=True)
        src = src[_o]
        dst = dst[_o]
        edge_attr_32 = 0.000196303 + 1.00016 * jax.random.normal(jax.random.fold_in(_gk, 12), (50000, 32), jnp.float32)
        edge_type_16 = jax.random.randint(jax.random.fold_in(_gk, 14), (50000,), 0, 16, jnp.int32)
        edge_type_8 = jax.random.randint(jax.random.fold_in(_gk, 15), (50000,), 0, 8, jnp.int32)
        return (x, src, dst, edge_attr_32, edge_type_16, edge_type_8)
    x, src, dst, edge_attr_32, edge_type_16, edge_type_8 = _rec_inputs()

    def _L0_gnn_setup():
        import jax, jax.numpy as jnp
        import numpy as np
        N_NODES = 50000
        N_EDGES = 25000
        D_IN = 64
        D_OUT = 64
        NUM_RELS = 16
        key = jax.random.key(seed)
        k1, k2, k3, k4, k5 = jax.random.split(key, 5)
        feat = jax.random.normal(k1, (N_NODES, D_IN), dtype=jnp.float32)
        weight = jax.random.normal(k2, (NUM_RELS, D_IN, D_OUT), dtype=jnp.float32) * 0.05
        src = jax.random.randint(k3, (N_EDGES,), 0, N_NODES, dtype=jnp.int32)
        dst = jax.random.randint(k4, (N_EDGES,), 0, N_NODES, dtype=jnp.int32)
        etypes = jax.random.randint(k5, (N_EDGES,), 0, NUM_RELS, dtype=jnp.int32)
        return {'feat': feat, 'weight': weight, 'src': src, 'dst': dst, 'etypes': etypes}
    _L0_gnn_all = _L0_gnn_setup()
    _L0_gnn_in = {k: v for k, v in _L0_gnn_all.items() if k in ('weight',)}
    del _L0_gnn_all

    def _L1_gnn_setup():
        import jax, jax.numpy as jnp
        import numpy as np
        N_NODES = 3125
        N_EDGES = 31250
        D_IN = 64
        D_HID = 64
        key = jax.random.key(seed)
        k1, k2, k3, k4, k5 = jax.random.split(key, 5)
        x = jax.random.normal(k1, (N_NODES, D_IN), dtype=jnp.float32)
        edge_index = jax.random.randint(k2, (2, N_EDGES), 0, N_NODES, dtype=jnp.int64)
        s = 1.0 / np.sqrt(D_IN)
        W_l = jax.random.normal(k3, (D_HID, D_IN), dtype=jnp.float32) * s
        b_l = jax.random.normal(k4, (D_HID,), dtype=jnp.float32) * 0.01
        W_r = jax.random.normal(k5, (D_HID, D_IN), dtype=jnp.float32) * s
        return {'x': x, 'edge_index': edge_index, 'W_l': W_l, 'b_l': b_l, 'W_r': W_r}
    _L1_gnn_all = _L1_gnn_setup()
    _L1_gnn_in = {k: v for k, v in _L1_gnn_all.items() if k in ('W_l', 'b_l', 'W_r')}
    del _L1_gnn_all

    def _L2_gnn_setup():
        import jax, jax.numpy as jnp
        import numpy as np
        N, E, H, ED = (50000, 25000, 64, 32)

        def _layernorm(h, gamma, beta, eps=1e-05):
            mu = jnp.mean(h, axis=-1, keepdims=True)
            var = jnp.mean(jnp.square(h - mu), axis=-1, keepdims=True)
            return (h - mu) * jax.lax.rsqrt(var + eps) * gamma + beta
        key = jax.random.key(seed)
        ks = jax.random.split(key, 16)
        s = lambda fan_in: 1.0 / np.sqrt(fan_in)
        inp = {'x': jax.random.normal(ks[0], (N, H), dtype=jnp.float32), 'edge_index': jax.random.randint(ks[1], (2, E), 0, N, dtype=jnp.int64), 'edge_attr': jax.random.normal(ks[2], (E, ED), dtype=jnp.float32), 'w1': jax.random.uniform(ks[3], (2 * H + ED, H), jnp.float32, -s(2 * H + ED), s(2 * H + ED)), 'b1': jnp.zeros((H,), jnp.float32), 'w2': jax.random.uniform(ks[4], (H, H), jnp.float32, -s(H), s(H)), 'b2': jnp.zeros((H,), jnp.float32), 'w3': jax.random.uniform(ks[5], (2 * H, H), jnp.float32, -s(2 * H), s(2 * H)), 'b3': jnp.zeros((H,), jnp.float32), 'w4': jax.random.uniform(ks[6], (H, H), jnp.float32, -s(H), s(H)), 'b4': jnp.zeros((H,), jnp.float32), 'gamma': jnp.ones((H,), jnp.float32), 'beta': jnp.zeros((H,), jnp.float32)}
        return inp
    _L2_gnn_all = _L2_gnn_setup()
    _L2_gnn_in = {k: v for k, v in _L2_gnn_all.items() if k in ('w1', 'b1', 'w2', 'b2', 'w3', 'b3', 'w4', 'b4', 'gamma', 'beta')}
    del _L2_gnn_all

    def _L3_gnn_setup():
        import jax, jax.numpy as jnp
        import numpy as np
        N_NODES = 50000
        N_EDGES = 25000
        IN_DIM = 64
        OUT_DIM = 64
        N_REL = 8
        N_RULES = 32
        N_ACTIVE = 4
        LN_EPS = 1e-05

        def _seg_softmax(scores, seg, num_segments):
            m = jax.ops.segment_max(scores, seg, num_segments=num_segments)
            e = jnp.exp(scores - m[seg])
            d = jax.ops.segment_sum(e, seg, num_segments=num_segments)
            return e / d[seg]
        key = jax.random.key(seed)
        ks = jax.random.split(key, 12)
        x = jax.random.normal(ks[0], (N_NODES, IN_DIM), dtype=jnp.float32)
        edge_index = jax.random.randint(ks[1], (2, N_EDGES), 0, N_NODES, dtype=jnp.int64)
        edge_type = jax.random.randint(ks[2], (N_EDGES,), 0, N_REL, dtype=jnp.int64)
        rule_ids = jax.random.randint(ks[3], (N_ACTIVE,), 0, N_RULES, dtype=jnp.int64)
        W_r = jax.random.normal(ks[4], (N_REL, IN_DIM, OUT_DIM), dtype=jnp.float32) * (2.0 / (IN_DIM + OUT_DIM)) ** 0.5
        Wq_w = jax.random.normal(ks[5], (IN_DIM, OUT_DIM), dtype=jnp.float32) * (1.0 / IN_DIM) ** 0.5
        Wq_bias = jnp.zeros((OUT_DIM,), dtype=jnp.float32)
        Wk_w = jax.random.normal(ks[6], (3 * IN_DIM, OUT_DIM), dtype=jnp.float32) * (1.0 / (3 * IN_DIM)) ** 0.5
        Wk_bias = jnp.zeros((OUT_DIM,), dtype=jnp.float32)
        rule_emb = jax.random.normal(ks[7], (N_RULES, IN_DIM), dtype=jnp.float32) * (2.0 / (N_RULES + IN_DIM)) ** 0.5
        bias = jnp.zeros((OUT_DIM,), dtype=jnp.float32)
        ln_g = jnp.ones((OUT_DIM,), dtype=jnp.float32)
        ln_b = jnp.zeros((OUT_DIM,), dtype=jnp.float32)
        return {'x': x, 'edge_index': edge_index, 'edge_type': edge_type, 'rule_ids': rule_ids, 'W_r': W_r, 'Wq_w': Wq_w, 'Wq_bias': Wq_bias, 'Wk_w': Wk_w, 'Wk_bias': Wk_bias, 'rule_emb': rule_emb, 'bias': bias, 'ln_g': ln_g, 'ln_b': ln_b}
    _L3_gnn_all = _L3_gnn_setup()
    _L3_gnn_in = {k: v for k, v in _L3_gnn_all.items() if k in ('rule_ids', 'W_r', 'Wq_w', 'Wq_bias', 'Wk_w', 'Wk_bias', 'rule_emb', 'bias', 'ln_g', 'ln_b')}
    del _L3_gnn_all
    return {'x': x, 'src': src, 'dst': dst, 'edge_attr_32': edge_attr_32, 'edge_type_16': edge_type_16, 'edge_type_8': edge_type_8, 'L0_gnn_weight': _L0_gnn_in['weight'], 'L1_gnn_W_l': _L1_gnn_in['W_l'], 'L1_gnn_b_l': _L1_gnn_in['b_l'], 'L1_gnn_W_r': _L1_gnn_in['W_r'], 'L2_gnn_w1': _L2_gnn_in['w1'], 'L2_gnn_b1': _L2_gnn_in['b1'], 'L2_gnn_w2': _L2_gnn_in['w2'], 'L2_gnn_b2': _L2_gnn_in['b2'], 'L2_gnn_w3': _L2_gnn_in['w3'], 'L2_gnn_b3': _L2_gnn_in['b3'], 'L2_gnn_w4': _L2_gnn_in['w4'], 'L2_gnn_b4': _L2_gnn_in['b4'], 'L2_gnn_gamma': _L2_gnn_in['gamma'], 'L2_gnn_beta': _L2_gnn_in['beta'], 'L3_gnn_rule_ids': _L3_gnn_in['rule_ids'], 'L3_gnn_W_r': _L3_gnn_in['W_r'], 'L3_gnn_Wq_w': _L3_gnn_in['Wq_w'], 'L3_gnn_Wq_bias': _L3_gnn_in['Wq_bias'], 'L3_gnn_Wk_w': _L3_gnn_in['Wk_w'], 'L3_gnn_Wk_bias': _L3_gnn_in['Wk_bias'], 'L3_gnn_rule_emb': _L3_gnn_in['rule_emb'], 'L3_gnn_bias': _L3_gnn_in['bias'], 'L3_gnn_ln_g': _L3_gnn_in['ln_g'], 'L3_gnn_ln_b': _L3_gnn_in['ln_b']}

def reference(x, src, dst, edge_attr_32, edge_type_16, edge_type_8, L0_gnn_weight, L1_gnn_W_l, L1_gnn_b_l, L1_gnn_W_r, L2_gnn_w1, L2_gnn_b1, L2_gnn_w2, L2_gnn_b2, L2_gnn_w3, L2_gnn_b3, L2_gnn_w4, L2_gnn_b4, L2_gnn_gamma, L2_gnn_beta, L3_gnn_rule_ids, L3_gnn_W_r, L3_gnn_Wq_w, L3_gnn_Wq_bias, L3_gnn_Wk_w, L3_gnn_Wk_bias, L3_gnn_rule_emb, L3_gnn_bias, L3_gnn_ln_g, L3_gnn_ln_b):
    import jax
    import jax.numpy as jnp

    def _L0_gnn_ref(feat, weight, src, dst, etypes):
        import jax, jax.numpy as jnp
        import numpy as np
        N_NODES = 50000
        N_EDGES = 25000
        D_IN = 64
        D_OUT = 64
        NUM_RELS = 16
        num_rels = weight.shape[0]
        h_src = feat[src]
        msg = jnp.zeros((h_src.shape[0], weight.shape[2]), dtype=feat.dtype)
        for r in range(num_rels):
            mask = etypes == r
            msg = msg + h_src * mask[:, None].astype(feat.dtype) @ weight[r]
        out = jax.ops.segment_sum(msg, dst, num_segments=feat.shape[0])
        return out

    def _L1_gnn_ref(x, edge_index, W_l, b_l, W_r):
        import jax, jax.numpy as jnp
        import numpy as np
        N_NODES = 3125
        N_EDGES = 31250
        D_IN = 64
        D_HID = 64
        src = edge_index[0]
        dst = edge_index[1]
        n = x.shape[0]
        msg = x[src]
        agg = jax.ops.segment_sum(msg, dst, num_segments=n)
        cnt = jax.ops.segment_sum(jnp.ones((src.shape[0], 1), x.dtype), dst, num_segments=n)
        mean = agg / jnp.maximum(cnt, 1.0)
        out = mean @ W_l.T + b_l + x @ W_r.T
        return jax.nn.elu(out)

    def _L2_gnn_ref(x, edge_index, edge_attr, w1, b1, w2, b2, w3, b3, w4, b4, gamma, beta):
        import jax, jax.numpy as jnp
        import numpy as np
        N, E, H, ED = (50000, 25000, 64, 32)

        def _layernorm(h, gamma, beta, eps=1e-05):
            mu = jnp.mean(h, axis=-1, keepdims=True)
            var = jnp.mean(jnp.square(h - mu), axis=-1, keepdims=True)
            return (h - mu) * jax.lax.rsqrt(var + eps) * gamma + beta
        source, target = (edge_index[0], edge_index[1])
        m_in = jnp.concatenate([x[source], x[target], edge_attr], axis=-1)
        m = jax.nn.silu(m_in @ w1 + b1) @ w2 + b2
        agg = jax.ops.segment_sum(m, target, num_segments=x.shape[0])
        u_in = jnp.concatenate([x, agg], axis=-1)
        upd = jax.nn.silu(u_in @ w3 + b3) @ w4 + b4
        return _layernorm(x + upd, gamma, beta)

    def _L3_gnn_ref(x, edge_index, edge_type, rule_ids, W_r, Wq_w, Wq_bias, Wk_w, Wk_bias, rule_emb, bias, ln_g, ln_b):
        import jax, jax.numpy as jnp
        import numpy as np
        N_NODES = 50000
        N_EDGES = 25000
        IN_DIM = 64
        OUT_DIM = 64
        N_REL = 8
        N_RULES = 32
        N_ACTIVE = 4
        LN_EPS = 1e-05

        def _seg_softmax(scores, seg, num_segments):
            m = jax.ops.segment_max(scores, seg, num_segments=num_segments)
            e = jnp.exp(scores - m[seg])
            d = jax.ops.segment_sum(e, seg, num_segments=num_segments)
            return e / d[seg]
        src, dst = (edge_index[0], edge_index[1])
        num_nodes, in_dim = x.shape
        num_rel, _, out_dim = W_r.shape
        x_src = x[src]
        q = x[dst] @ Wq_w + Wq_bias
        rel_emb = W_r.mean(axis=-1)[edge_type]
        Wk1, Wk2, Wk3 = (Wk_w[:in_dim], Wk_w[in_dim:2 * in_dim], Wk_w[2 * in_dim:])
        key_base = x_src @ Wk1 + rel_emb @ Wk2 + Wk_bias
        h_R = rule_emb[rule_ids]
        key_rule = h_R @ Wk3
        scale = 1.0 / out_dim ** 0.5
        score_base = jnp.einsum('eo,eo->e', q, key_base)
        score_rule = jnp.einsum('eo,ro->er', q, key_rule)
        scores = (score_base[:, None] + score_rule) * scale
        attn = jax.vmap(lambda s: _seg_softmax(s, dst, num_nodes), in_axes=1, out_axes=1)(scores)
        mean_attn = attn.mean(axis=1)
        msg = jnp.zeros((x_src.shape[0], out_dim), dtype=x.dtype)
        for r in range(num_rel):
            msg = jnp.where((edge_type == r)[:, None], x_src @ W_r[r], msg)
        out = jax.ops.segment_sum(msg * mean_attn[:, None], dst, num_segments=num_nodes)
        out = out + bias
        mu = out.mean(axis=-1, keepdims=True)
        var = ((out - mu) ** 2).mean(axis=-1, keepdims=True)
        out = (out - mu) * jax.lax.rsqrt(var + LN_EPS) * ln_g + ln_b
        return jax.nn.relu(out)
    edge_index = jnp.stack([src, dst])
    h = jnp.maximum(_layernorm(x, axis=-1), 0.0)
    x = x + _L0_gnn_ref(h, L0_gnn_weight, src, dst, edge_type_16)
    h = jnp.maximum(_layernorm(x, axis=-1), 0.0)
    x = x + _L1_gnn_ref(h, edge_index, L1_gnn_W_l, L1_gnn_b_l, L1_gnn_W_r)
    h = jnp.maximum(_layernorm(x, axis=-1), 0.0)
    x = x + _L2_gnn_ref(h, edge_index, edge_attr_32, L2_gnn_w1, L2_gnn_b1, L2_gnn_w2, L2_gnn_b2, L2_gnn_w3, L2_gnn_b3, L2_gnn_w4, L2_gnn_b4, L2_gnn_gamma, L2_gnn_beta)
    h = jnp.maximum(_layernorm(x, axis=-1), 0.0)
    x = x + _L3_gnn_ref(h, edge_index, edge_type_8, L3_gnn_rule_ids, L3_gnn_W_r, L3_gnn_Wq_w, L3_gnn_Wq_bias, L3_gnn_Wk_w, L3_gnn_Wk_bias, L3_gnn_rule_emb, L3_gnn_bias, L3_gnn_ln_g, L3_gnn_ln_b)
    return x

_drawn_inputs = setup_inputs


def setup_inputs(seed=0):
    import zlib

    import numpy as np

    out = dict(_drawn_inputs(seed))
    spreads = {'L2_gnn_b1': (0.0, 0.303),
     'L2_gnn_b2': (0.0, 0.1),
     'L2_gnn_b3': (0.0, 0.488),
     'L2_gnn_b4': (0.0, 0.1),
     'L2_gnn_gamma': (1.0, 0.2),
     'L2_gnn_beta': (0.0, 0.1),
     'L3_gnn_Wq_bias': (0.0, 0.8),
     'L3_gnn_Wk_bias': (0.0, 0.8),
     'L3_gnn_bias': (0.0, 0.1),
     'L3_gnn_ln_g': (1.0, 0.2),
     'L3_gnn_ln_b': (0.0, 0.306)}
    factors = {'L1_gnn_b_l': 8.0, 'L3_gnn_rule_emb': 8.0}
    for name, (base, spread) in spreads.items():
        noise = np.random.default_rng([zlib.crc32(name.encode()), seed]).standard_normal(out[name].shape)
        drawn = base * np.exp(spread * noise) if base else spread * noise
        out[name] = jnp.asarray(drawn.astype(out[name].dtype))
    for name, factor in factors.items():
        out[name] = (out[name] * factor).astype(out[name].dtype)
    return out
```

```python
import concourse.bass as bass
from concourse import mybir
from contextlib import ExitStack

P = 128
SG = 8


def network(nc, a, out, N, E):
    fp32, i32, bf16 = mybir.dt.float32, mybir.dt.int32, mybir.dt.bfloat16
    ALU, ACT = mybir.AluOpType, mybir.ActivationFunctionType
    AX = mybir.AxisListType.X
    PE_ = mybir.EngineType.PE
    SP_ = mybir.EngineType.SP

    D = a["x"].shape[1]
    ED = a["edge_attr_32"].shape[1]
    R0 = a["L0_gnn_weight"].shape[0]
    R3 = a["L3_gnn_W_r"].shape[0]
    NR = a["L3_gnn_rule_ids"].shape[0]
    TE = -(-E // P)
    TN = -(-N // P)
    SLOTS = -(-(TE + TN - 1) // (2 * SG)) * 2 * SG
    G = SLOTS // SG
    SC = -(-SLOTS // P)
    NT = TN + 1
    assert NT % 2 == 0 and SLOTS - (TE + TN - 1) <= 1 and G % 2 == 0
    M = NT // 2
    C = NT * D
    ELAST = E - (TE - 1) * P
    NLAST = N - (TN - 1) * P
    EPS = 1e-5

    ctx = ExitStack()
    with ctx:
        def sb(name, shape, dt=fp32):
            return ctx.enter_context(nc.sbuf_tensor(name, shape, dt))

        def sem(name):
            return ctx.enter_context(nc.semaphore(name))

        def dram(name, shape, dt=fp32):
            return nc.dram_tensor(name, shape, dt, kind="Internal").ap()

        pack_d = dram("edge_pack", (TE, 4 * P), i32)
        dst_d = dram("dst_shifted", (TE + 1, P), i32)
        ea_d = dram("edge_attr_padded", (TE * P, ED))
        table0_d = dram("table0", (NT * P, R0 * D))
        table1_d = dram("table1", (NT * P, D))
        table2_d = dram("table2", (NT * P, D))
        table3_d = dram("table3", (NT * P, R3 * 2 * D))

        values = sb("values", [P, SLOTS, D])
        flat = values[:, :, :].rearrange("p s d -> p (s d)")
        taken = [0]

        def early(rows_, shape, dt=fp32):
            n = 1
            for k in shape:
                n *= k
            x = flat[0:rows_, taken[0]:taken[0] + n]
            taken[0] += n
            assert taken[0] <= SLOTS * D
            if dt != fp32:
                x = x.bitcast(dt)
            if len(shape) == 1:
                return x
            names = "abcd"[:len(shape)]
            return x.rearrange(f"p ({' '.join(names)}) -> p {' '.join(names)}", **dict(zip(names, shape)))

        ident = sb("ident", [P, P])
        ident_h = sb("ident_h", [P, P], bf16)
        iota_n = sb("iota_n", [P, P])
        iota_slot = sb("iota_slot", [P, SC])
        zeros = sb("zeros", [P, 512])
        ones = sb("ones", [P, 1])
        fill_i = early(1, [2 * P], i32)
        zero_i = early(1, [P], i32)

        w0 = early(P, [R0, D])
        wl_rows = early(D, [2, D])
        wr_rows = early(D, [2, D])
        wlT = early(P, [D])
        wrT = early(P, [D])
        w1ab = early(P, [2, D])
        w1c = early(P, [4, D])
        w2 = early(P, [D])
        w3 = early(P, [2, D])
        w4 = early(P, [D])
        wq = sb("wq", [P, D])
        wr3 = sb("wr3", [P, R3, D])
        wk1 = sb("wk1", [P, D])
        wk2 = sb("wk2", [D, D])
        wk3 = sb("wk3", [D, 2, D])
        ROWS = ["L1_gnn_b_l", "L2_gnn_b1", "L2_gnn_b2", "L2_gnn_b3", "L2_gnn_b4", "L2_gnn_gamma", "L2_gnn_beta",
                "L3_gnn_Wq_bias", "L3_gnn_Wk_bias", "L3_gnn_bias", "L3_gnn_ln_g", "L3_gnn_ln_b"]
        rows = sb("rows", [P, len(ROWS), D])
        rule_ids = sb("rule_ids", [NR, 1], i32)
        rule_rows = sb("rule_rows", [NR, D])
        ruleT = sb("ruleT", [D, NR])
        key_rule = sb("key_rule", [P, NR])
        rel_sum = sb("rel_sum", [P, R3])
        rel_key = sb("rel_key", [P, R3, D])

        def row(name):
            return rows[:, ROWS.index(name), :].unsqueeze(1).broadcast_to([P, NT, D])

        dst_rows = early(P, [SC, P], i32)
        reach_i = sb("reach_i", [P, SC], i32)
        reach = sb("reach", [P, SC])
        slot_t = sb("slot_t", [P, SC])
        slot_n = sb("slot_n", [P, SC])
        slot_n128 = sb("slot_n128", [P, SC])
        slot_ti = sb("slot_ti", [P, SC], i32)
        NBITS = 8
        n_row = sb("n_row", [1, SC * P // SG], i32)
        n_slots = early(1, [SC * P // SG, SG])
        n_steps = early(1, [SC * P // SG, SG - 1])
        n_words = early(1, [SC * P // SG])
        drel = sb("drel", [P, SLOTS])
        idx0 = early(P, [SLOTS], i32)
        idx1 = early(P, [SLOTS], i32)
        idx3 = sb("idx3", [P, SLOTS], i32)
        seg_start = sb("seg_start", [P, SC, P])
        seg_end = sb("seg_end", [P, SC, P])
        valid = sb("valid", [P, SC, P])

        xs = sb("xs", [P, NT, D])
        h = sb("h", [P, NT, D])
        u = sb("u", [P, NT, D])
        v = sb("v", [P, NT, D])
        mean = sb("mean", [P, NT])
        var = sb("var", [P, NT])
        std = sb("std", [P, NT])
        cnt = sb("cnt", [P, NT])
        rcnt = sb("rcnt", [P, NT])
        hT = sb("hT", [P, M, P])
        uT = early(P, [M, P])
        qn = sb("qn", [P, 3, NT, D + NR], bf16)

        idx_ring = sb("idx_ring", [P, 2, SG], i32)
        got = sb("got", [P, 2, SG, 2 * D])
        got1 = [got[:, b, :, :].rearrange("p s d -> p (s d)")[:, 0:SG * D].rearrange("p (s d) -> p s d", s=SG) for b in range(2)]
        oh = sb("oh", [P, 2, SG, P])
        oh_bytes = sb("oh_bytes", [P, 2 * SG * P])
        half = SG * P
        ohb = oh_bytes[:, 0:half].bitcast(bf16).rearrange("p (b s k) -> p b s k", b=2, s=SG)
        ohT = oh_bytes[:, half:2 * half].bitcast(bf16).rearrange("p (b s k) -> p b s k", b=2, s=SG)
        ea = early(P, [2, SG * ED])
        eaT = early(P, [2, 2, P])
        msg = sb("msg", [P, 2, SG, D])
        stage = early(P, [4, R0 * D])
        base = sb("base", [P, SC * P])
        rule_e = sb("rule_e", [P, SC * P, NR])

        pack = early(P, [SC, 4, P], i32)
        dprev = early(P, [SC, P], i32)
        dnext = early(P, [SC, P], i32)
        work = [early(P, [SC, P]) for _ in range(4)]

        ps = ctx.enter_context(nc.psum_tensor("ps", [P, 4096], fp32))
        acc = ps[:, 0:2048]
        aux = ps[:, 2048:4096]
        tp = [ps[:, 2048:2560], ps[:, 2560:3072]]
        eb = [ps[:, 3072:3584], ps[:, 3584:4096]]

        def rows_in(t, q):
            return t.rearrange("p a b -> p (a b)")[:, q * SC * P:(q + 1) * SC * P].rearrange("p (c k) -> p c k", c=SC)

        keep_s, keep_e, open_s, open_e, f1, f2, f3 = [rows_in(t[:, :, :], q) for t, q in ((u, 0), (u, 1), (u, 2), (v, 0), (v, 1), (v, 2), (hT, 0))]
        prob = oh[:, :, :, :].rearrange("p b s k -> p (b s k)").rearrange("p (r c k) -> p r c k", r=NR, c=SC)
        total = oh_bytes[:, :].rearrange("p (r c k) -> p r c k", r=NR, c=SC)
        row_keep = sb("row_keep", [P, 2, SC, NR])
        row_end = sb("row_end", [P, SC, NR])
        idle = got[:, :, :, :].rearrange("p b s d -> p (b s d)")
        carry_keep = idle[0:NR, 0:2 * SC * P].rearrange("r (e l) -> r e l", e=2)
        carry_pen = idle[0:1, 2 * SC * P:3 * SC * P]
        carry = msg[:, :, :, :].rearrange("p b s d -> p (b s d)")[0:NR, 0:SC * P + 1]
        carry_col = sb("carry_col", [P, SC, NR])

        def products(x, w=D):
            return x.rearrange("p (q y) -> p q y", q=2)[:, :, 0:M * w].rearrange("p q (m d) -> p q m d", d=w)

        def by_parity(t):
            return t.rearrange("p (m q) d -> p q m d", q=2)

        def row2(name):
            return rows[:, ROWS.index(name), :].unsqueeze(1).unsqueeze(1).broadcast_to([P, 2, M, D])

        def tiles(x):
            return x[:, 0:C].rearrange("p (t d) -> p t d", t=NT)

        S = {}

        def s(name):
            if name not in S:
                S[name] = sem(name)
            return S[name]

        for name in ("init", "const", "scratch", "x_in", "weights", "dst_in", "dve"):
            s(name)
        gat = [s("gathered0"), s("gathered1")]
        eas = [s("ea_in0"), s("ea_in1")]
        tab = [s(f"table_out{b}") for b in range(4)]

        INIT = 11

        def slot_tiles(engine, g):
            word = nc.values_load(n_row[0:1, bass.ds(g, 1)], engines=[engine], min_val=0, max_val=(1 << (NBITS + SG - 1)) - 1,
                                  skip_runtime_bounds_check_because="counted on the chip from the destinations")
            n = [nc.snap(word & ((1 << NBITS) - 1), min_val=0, max_val=NT - 1)]
            for j in range(SG - 1):
                n.append(nc.snap(n[-1] + ((word >> (NBITS + j)) & 1), min_val=0, max_val=NT - 1))
            return n

        def tables(eng, l, half):
            for b in range(4):
                half(l, 0, b, l == 0)
            with eng.Fori(1, NT // 4) as it:
                for b in range(4):
                    half(l, it, b)
            for n in range(NT // 4 * 4, NT):
                half(l, n // 4, n % 4)

        def skewed(eng, before, after):
            before(0, 0)
            with eng.Fori(0, G // 2 - 1) as it:
                before(it, 1)
                after(it, 0)
                before(it + 1, 0)
                after(it, 1)
            before(G // 2 - 1, 1)
            after(G // 2 - 1, 0)
            after(G // 2 - 1, 1)

        NW = 0
        block = ctx.enter_context(nc.Block())
        PER = SG * 16

        WEIGHTS = []

        def weight(dst, src):
            WEIGHTS.append((dst, src))
        for q in range(2):
            hf = slice(q * D, (q + 1) * D)
            weight(w0[hf], a["L0_gnn_weight"].rearrange("r i o -> i r o"))
            weight(wl_rows[:, q, :], a["L1_gnn_W_l"])
            weight(wr_rows[:, q, :], a["L1_gnn_W_r"])
            weight(w1ab[hf], a["L2_gnn_w1"][0:2 * D, :].rearrange("(s i) o -> i s o", s=2))
            weight(w2[hf], a["L2_gnn_w2"])
            weight(w3[hf], a["L2_gnn_w3"].rearrange("(s i) o -> i s o", s=2))
            weight(w4[hf], a["L2_gnn_w4"])
            weight(wq[hf], a["L3_gnn_Wq_w"])
            weight(wr3[hf], a["L3_gnn_W_r"].rearrange("r i o -> i r o"))
            weight(wk1[hf], a["L3_gnn_Wk_w"][0:D, :])
            weight(wk3[:, q, :], a["L3_gnn_Wk_w"][2 * D:3 * D, :])
        weight(wk2[:], a["L3_gnn_Wk_w"][D:2 * D, :])
        for j in range(4):
            weight(w1c[j * ED:(j + 1) * ED, j, :], a["L2_gnn_w1"][2 * D:2 * D + ED, :])
        for j, name in enumerate(ROWS):
            weight(rows[:, j, :], a[name].unsqueeze(0).broadcast_to([P, D]))
        weight(rule_ids[:], a["L3_gnn_rule_ids"].unsqueeze(1))
        NW = 16 * len(WEIGHTS)
        SCR = 16 * 13

        @block.sync
        def _(sp):
            full = (TE - 1) * P
            sp.wait_ge(s("init"), INIT)
            sp.dma_start(dst_rows[:, 0:SC - 1, :], a["dst"][0:(SC - 1) * P * P].rearrange("(c p k) -> p c k", p=P, k=P)).then_inc(s("dst_in"), 16)
            sp.dma_start(dst_rows[0:TE - 1 - (SC - 1) * P, SC - 1, :],
                         a["dst"][(SC - 1) * P * P:full].rearrange("(p k) -> p k", k=P)).then_inc(s("dst_in"), 16)
            for j, name in enumerate(("src", "dst", "edge_type_16", "edge_type_8")):
                sp.dma_start(pack_d[0:TE - 1, j * P:(j + 1) * P], a[name][0:full].rearrange("(t k) -> t k", k=P)).then_inc(s("scratch"), 16)
                sp.dma_start(pack_d[TE - 1:TE, j * P:j * P + ELAST], a[name][full:E].unsqueeze(0)).then_inc(s("scratch"), 16)
            for j, f in enumerate((zero_i, fill_i, zero_i, zero_i)):
                sp.dma_start(pack_d[TE - 1:TE, j * P + ELAST:(j + 1) * P], f[0:1, 0:P - ELAST]).then_inc(s("scratch"), 16)
            dflat = dst_d.rearrange("t k -> (t k)")
            sp.dma_start(dflat[1:E + 1].rearrange("(p k) -> p k", k=E // 16), a["dst"].rearrange("(p k) -> p k", k=E // 16)).then_inc(s("scratch"), 16)
            sp.wait_ge(s("init"), INIT)
            sp.dma_start(xs[:, 0:TN - 1, :], a["x"][0:(TN - 1) * P, :].rearrange("(t p) d -> p t d", p=P)).then_inc(s("x_in"), 16)
            sp.dma_start(xs[0:NLAST, TN - 1, :], a["x"][(TN - 1) * P:N, :]).then_inc(s("x_in"), 16)
            for d, w in WEIGHTS:
                sp.dma_start(d, w).then_inc(s("weights"), 16)
            sp.dma_start(ea_d[0:E, :].rearrange("(p k) d -> p (k d)", p=16), a["edge_attr_32"].rearrange("(p k) d -> p (k d)", p=16)).then_inc(s("ea_scratch"), 16)
            sp.dma_start(ea_d[E:TE * P, :].rearrange("n d -> (n d)").unsqueeze(0), zeros[0:1, :].unsqueeze(1).broadcast_to([1, (TE * P - E) * ED // 512, 512])).then_inc(s("ea_scratch"), 16)

            def table_out(l, n, b, table):
                sp.wait_ge(s("tabA"), NT * l + n + 1)
                sp.wait_ge(s("tabB"), NT * l + n + 1)
                sp.dma_start(table[bass.ds(n * P, P), :], stage[:, b, :]).then_inc(tab[b], 16)

            def tables_out(l, table):
                with sp.Fori(0, NT // 4) as it:
                    for b in range(4):
                        table_out(l, 4 * it + b, b, table)
                for n in range(NT // 4 * 4, NT):
                    table_out(l, n, n % 4, table)

            tables_out(0, table0_d)
            for l, (src_, table) in enumerate(((h, table1_d), (u, table2_d))):
                sp.wait_ge(s("plain_table"), l + 1)
                sp.dma_start(table.rearrange("(t p) d -> p t d", p=P), src_[:]).then_inc(s("plain_table_out"), 16)

            def ea_in(g, b):
                n = slot_tiles(SP_, g)
                t = [nc.snap(g * SG + j - n[j], min_val=0, max_val=TE - 1) for j in range(SG)]
                sp.wait_ge(s("eaT_ps"), g + 1)
                for j in range(SG):
                    sp.dma_start(ea[:, b, j * ED:(j + 1) * ED], ea_d[bass.ds(t[j] * P, P), :]).then_inc(eas[b], 16)

            sp.wait_ge(s("ea_scratch"), 32)
            sp.wait_ge(s("n_row"), 1)
            with sp.Fori(0, G // 2) as it:
                for b in range(2):
                    ea_in(2 * it + b, b)

            tables_out(1, table3_d)

            sp.wait_ge(s("x_done"), 1)
            sp.dma_start(out[0:(TN - 1) * P, :].rearrange("(t p) d -> p t d", p=P), xs[:, 0:TN - 1, :]).then_inc(s("stored"), 16)
            sp.dma_start(out[(TN - 1) * P:N, :], xs[0:NLAST, TN - 1, :]).then_inc(s("stored"), 16)
            sp.wait_ge(s("stored"), 32)

        @block.gpsimd
        def _(pool):
            nc.gpsimd.iota(iota_n[:], pattern=[[1, P]], base=0, channel_multiplier=0, allow_small_or_imprecise_dtypes=True).then_inc(s("const"), 1)
            nc.gpsimd.iota(iota_slot[:], pattern=[[P, SC]], base=0, channel_multiplier=1, allow_small_or_imprecise_dtypes=True).then_inc(s("const"), 1)
            nc.gpsimd.memset(ident[:], 0.0).then_inc(s("ident0"), 1)
            pool.wait_ge(s("ident0"), 1)
            nc.gpsimd.affine_select(out=ident[:], in_=ident[:], compare_op=ALU.not_equal, fill=1.0, base=0,
                                    pattern=[[-1, P]], channel_multiplier=1).then_inc(s("const"), 1)
            pool.wait_ge(s("init"), INIT)
            dflat = dst_d.rearrange("t k -> (t k)")
            pool.dma_start(dflat[0:1].unsqueeze(0), fill_i[0:1, 0:1]).then_inc(s("scratch_fill"), 16)
            pool.dma_start(dflat[E + 1:(TE + 1) * P].unsqueeze(0), fill_i[0:1, 0:(TE + 1) * P - E - 1]).then_inc(s("scratch_fill"), 16)
            pool.wait_ge(s("scratch_fill"), 32)
            pool.wait_ge(s("scratch"), SCR)
            pool.wait_ge(s("slot_t"), 1)
            for c in range(SC):
                n = min(P, SLOTS - c * P)
                at_ = bass.IndirectOffsetOnAxis(ap=slot_ti[0:n, c:c + 1], axis=0)
                nc.gpsimd.indirect_dma_start(pack[0:n, c, :, :].rearrange("p a k -> p (a k)"), None, pack_d[:, :], at_).then_inc(s("packed"), 16)
                nc.gpsimd.indirect_dma_start(dprev[0:n, c, :], None, dst_d[:, :], at_).then_inc(s("packed"), 16)
                nc.gpsimd.indirect_dma_start(dnext[0:n, c, :], None, dst_d[:, :], at_, element_offset=2).then_inc(s("packed"), 16)
            pool.wait_ge(s("weights"), NW)
            nc.gpsimd.indirect_dma_start(rule_rows[:], None, a["L3_gnn_rule_emb"][:, :],
                                         bass.IndirectOffsetOnAxis(ap=rule_ids[:, 0:1], axis=0)).then_inc(s("rule_rows"), 16)

            def gather(l, table, dest):
                with pool.Fori(0, G // 2) as it:
                    for b in range(2):
                        pool.wait_ge(s("idx"), l * G + 2 * it + b + 1)
                        pool.sem_inc(s("gathers_begun"), 1)
                        for j in range(SG):
                            nc.gpsimd.indirect_dma_start(dest(b, j), None, table, bass.IndirectOffsetOnAxis(ap=idx_ring[:, b, j:j + 1], axis=0)).then_inc(gat[b], 16)

            for b in range(4):
                pool.wait_ge(tab[b], 16 * len(range(b, NT, 4)))
            gather(0, table0_d.rearrange("n (r d) -> (n r) d", d=D), lambda b, j: got1[b][:, j, :])
            pool.wait_ge(s("plain_table_out"), 16)
            gather(1, table1_d[:, :], lambda b, j: got1[b][:, j, :])
            pool.wait_ge(s("plain_table_out"), 32)
            gather(2, table2_d[:, :], lambda b, j: got1[b][:, j, :])
            for b in range(4):
                pool.wait_ge(tab[b], 32 * len(range(b, NT, 4)))
            gather(3, table3_d.rearrange("n (r d) -> (n r) d", d=2 * D), lambda b, j: got[:, b, j, :])

        @block.vector
        def _(dve):
            V = nc.vector
            chain = [0]

            def link(ins):
                chain[0] += 1
                ins.then_inc(s("dve"), 1)
                dve.wait_ge(s("dve"), chain[0])

            V.memset(zeros[:], 0.0).then_inc(s("init"), 1)
            V.memset(ones[:], 1.0).then_inc(s("init"), 1)
            V.memset(fill_i[:], -1).then_inc(s("init"), 1)
            V.memset(zero_i[:], 0).then_inc(s("init"), 1)
            V.memset(xs[:, TN - 1:NT, :], 0.0).then_inc(s("init"), 1)
            V.memset(w1c[:], 0.0).then_inc(s("init"), 1)
            V.memset(pack[:, SC - 1, :, :], 0).then_inc(s("init"), 1)
            V.memset(dprev[:, SC - 1, :], 0).then_inc(s("init"), 1)
            V.memset(dnext[:, SC - 1, :], 0).then_inc(s("init"), 1)
            V.memset(dst_rows[:, SC - 1, :], 0).then_inc(s("init"), 1)
            V.memset(base[:, SLOTS:], 0.0).then_inc(s("init"), 1)
            link(V.memset(rule_e[:, SLOTS:, :], 0.0))

            dve.wait_ge(s("dst_in"), 32)
            dve.wait_ge(s("const"), 3)
            link(V.tensor_scalar(reach_i[:], dst_rows[:, :, P - 1], 7, None, ALU.arith_shift_right))
            link(V.tensor_tensor(reach[:], reach_i[:], iota_slot[:], ALU.add))
            link(V.tensor_scalar(slot_t[:], iota_slot[:], float(TE - 1), 1e6, ALU.is_ge, ALU.mult))
            V.tensor_tensor(reach[:], reach[:], slot_t[:], ALU.add).then_inc(s("reach"), 1)
            dve.wait_ge(s("reach_row"), 1)
            link(V.tensor_copy(ident_h[:], ident[:]))
            for c in range(SC):
                link(V.tensor_scalar(work[0][:, :, :].rearrange("p c k -> p (c k)"), aux[:, 0:SC * P], iota_slot[:, c:c + 1], None, ALU.is_lt, ALU.add, accum_out=slot_t[:, c:c + 1]))
            link(V.tensor_copy(slot_ti[:], slot_t[:]))
            link(V.tensor_tensor(slot_n[:], iota_slot[:], slot_t[:], ALU.subtract))
            V.tensor_scalar(slot_n128[:], slot_n[:], float(P), None, ALU.mult).then_inc(s("slot_t"), 1)
            dve.wait_ge(s("rows_ps"), 1)
            n_ps = aux[0:1, 512:512 + SC * P].rearrange("o (g j) -> o g j", j=SG)
            link(V.tensor_copy(n_slots, n_ps))
            link(V.tensor_copy(n_words, n_slots[:, :, 0]))
            link(V.tensor_tensor(n_steps, n_slots[:, :, 1:SG], n_slots[:, :, 0:SG - 1], ALU.subtract))
            for j in range(SG - 1):
                link(V.scalar_tensor_tensor(n_words, n_steps[:, :, j], float(1 << (NBITS + j)), n_words, ALU.mult, ALU.add))
            V.tensor_copy(n_row[:], n_words).then_inc(s("n_row"), 1)
            dve.wait_ge(s("packed"), 16 * 3 * SC)
            dve.wait_ge(s("slot_t"), 1)
            src_, dst_, t16, t8 = (pack[:, :, j, :] for j in range(4))
            link(V.scalar_tensor_tensor(work[0], src_, float(R0), t16, ALU.mult, ALU.add))
            link(V.tensor_copy(work[1], src_))
            link(V.scalar_tensor_tensor(work[2], src_, float(R3), t8, ALU.mult, ALU.add))
            for c in range(SC):
                link(V.tensor_scalar(work[3][:, c, :], dst_[:, c, :], slot_n128[:, c:c + 1], None, ALU.subtract))
            dve.sem_inc(s("work"), 1)
            link(V.tensor_scalar(valid[:], work[3], 0.0, None, ALU.is_ge))
            link(V.tensor_scalar(seg_start[:], work[3], float(P - 1), None, ALU.is_le))
            link(V.tensor_tensor(valid[:], valid[:], seg_start[:], ALU.mult))
            for seg, other in ((seg_start, dprev), (seg_end, dnext)):
                link(V.tensor_tensor(seg[:], dst_, other, ALU.not_equal))
                link(V.tensor_tensor(seg[:], seg[:], valid[:], ALU.mult))
            for j, t in enumerate((idx0, idx1, idx3, drel)):
                dve.wait_ge(s("work_T"), j + 1)
                link(V.tensor_copy(t[:], aux[:, 512 * j:512 * j + SLOTS]))
            dve.sem_inc(s("tables_made"), 1)
            dve.wait_ge(s("wT_ps"), 2)
            for q, wT in enumerate((wlT, wrT)):
                link(V.tensor_copy(wT[:], aux[:, q * D:(q + 1) * D]))
            dve.sem_inc(s("wT_sb"), 1)

            sums = [0]

            def normed(x, name=None):
                link(V.tensor_reduce(mean[:], x, AX, ALU.add))
                link(V.tensor_scalar(mean[:], mean[:], 1.0 / D, None, ALU.mult))
                link(V.tensor_tensor(v[:], x, mean[:].unsqueeze(2).broadcast_to([P, NT, D]), ALU.subtract))
                link(V.tensor_tensor(u[:], v[:], v[:], ALU.mult))
                link(V.tensor_reduce(var[:], u[:], AX, ALU.add))
                V.tensor_scalar(var[:], var[:], 1.0 / D, EPS, ALU.mult, ALU.add).then_inc(s("var"), 1)
                sums[0] += 1
                dve.wait_ge(s("std"), sums[0])
                link(V.reciprocal(std[:], std[:]))

            def pre_norm():
                normed(xs[:])
                V.scalar_tensor_tensor(h[:], v[:], 0.0, std[:].unsqueeze(2).broadcast_to([P, NT, D]), ALU.max, ALU.mult).then_inc(s("h"), 1)

            def build_onehots(l, g, b):
                dests = [ohb] * (l in (2, 3)) + [oh] * (l != 3)
                for dest in dests:
                    last = V.tensor_tensor(dest[:, b], iota_n[:].unsqueeze(1).broadcast_to([P, SG, P]),
                                           drel[:, bass.ds(g * SG, SG)].unsqueeze(2).broadcast_to([P, SG, P]), ALU.is_equal)
                last.then_inc(s("oh"), 1)

            def three_parts(x, rest, cols, signal):
                link(V.tensor_copy(qn[:, 0, :, cols], x))
                link(V.tensor_tensor(rest, x, qn[:, 0, :, cols], ALU.subtract))
                link(V.tensor_copy(qn[:, 1, :, cols], rest))
                V.tensor_tensor(qn[:, 2, :, cols], rest, qn[:, 1, :, cols], ALU.subtract).then_inc(s(signal), 1)

            def stage_indices(idx, g, b):
                V.tensor_copy(idx_ring[:, b, :], idx[:, bass.ds(g * SG, SG)]).then_inc(s("idx"), 1)

            dve.wait_ge(s("x_in"), 32)
            pre_norm()
            evens = [0]

            def table_half(l, q, b, first=False):
                n = 4 * q + b
                """Half of a node tile's table rows from PSUM: VectorE's half."""
                dve.wait_ge(s("tab_ps"), NT * l + n + 1)
                if not first:
                    dve.wait_ge(tab[b], 16 * (l * len(range(b, NT, 4)) + q))
                if l == 0:
                    V.tensor_copy(stage[:, b, 0:512], acc[:, (b % 2) * 1024:(b % 2) * 1024 + 512]).then_inc(s("tabA"), 1)
                else:
                    V.tensor_tensor(stage[:, b, :].rearrange("p (r q d) -> p r q d", q=2, d=D)[:, :, 1, :],
                                    acc[:, (b % 2) * 1024 + 512:(b % 2) * 1024 + 512 + D].unsqueeze(1).broadcast_to([P, R3, D]),
                                    rel_key[:], ALU.add).then_inc(s("tabA"), 1)

            tables(dve, 0, table_half)

            def simple_loop(l, idx):
                with dve.Fori(0, G // 2) as it:
                    for b in range(2):
                        g = 2 * it + b
                        dve.wait_ge(s("used"), l * G + g + 1)
                        stage_indices(idx, g, b)
                        build_onehots(l, g, b)

            simple_loop(0, idx0)
            dve.wait_ge(s("used"), 2 + G)
            link(V.tensor_tensor(xs[:], xs[:], tiles(acc), ALU.add))
            link(V.tensor_copy(cnt[:], acc[:, C:C + NT]))
            link(V.tensor_scalar(rcnt[:], cnt[:], 1.0, None, ALU.max))
            link(V.reciprocal(rcnt[:], rcnt[:]))
            pre_norm()
            dve.wait_ge(s("h"), 2)
            dve.sem_inc(s("plain_table"), 1)
            simple_loop(1, idx1)
            dve.wait_ge(s("used"), 2 + 2 * G)
            V.tensor_tensor(u[:], tiles(acc), rcnt[:].unsqueeze(2).broadcast_to([P, NT, D]), ALU.mult).then_inc(s("u"), 1)
            dve.wait_ge(s("node_mm"), 1 * M)
            link(V.tensor_tensor(by_parity(u[:]), products(acc), row2("L1_gnn_b_l"), ALU.add))
            V.tensor_scalar(v[:], u[:], 0.0, None, ALU.min).then_inc(s("elu_in"), 1)
            link(V.scalar_tensor_tensor(u[:], u[:], 0.0, xs[:], ALU.max, ALU.add))
            dve.wait_ge(s("elu_exp"), 1)
            link(V.scalar_tensor_tensor(xs[:], v[:], -1.0, u[:], ALU.add, ALU.add))
            pre_norm()
            dve.wait_ge(s("node_mm"), 2 * M)
            V.tensor_copy(by_parity(u[:]), products(acc)).then_inc(s("plain_table"), 1)
            link(V.tensor_tensor(by_parity(v[:]), products(aux), row2("L2_gnn_b1"), ALU.add))
            three_parts(v[:], v[:], slice(0, D), "qn")

            def before2(k, b):
                g = 2 * k + b
                dve.wait_ge(s("used"), 2 * G + g + 1)
                stage_indices(idx1, g, b)
                build_onehots(2, g, b)

            def after2(k, b):
                g = 2 * k + b
                dve.wait_ge(s("eb_ps"), g + 1)
                dve.wait_ge(gat[b], 2 * (G // 2) * PER + (k + 1) * PER)
                V.tensor_tensor(got1[b], eb[b].rearrange("p (s d) -> p s d", s=SG), got1[b], ALU.add).then_inc(s("edge_sum"), 1)

            skewed(dve, before2, after2)
            dve.wait_ge(s("used"), 2 + 3 * G)
            V.tensor_copy(u[:], tiles(acc)).then_inc(s("u"), 1)
            dve.wait_ge(s("node_mm"), 3 * M)
            link(V.tensor_tensor(v[:], cnt[:].unsqueeze(2).broadcast_to([P, NT, D]), row("L2_gnn_b2"), ALU.mult))
            V.tensor_tensor(by_parity(u[:]), by_parity(v[:]), products(acc), ALU.add).then_inc(s("u"), 1)
            dve.wait_ge(s("node_mm"), 4 * M)
            V.tensor_tensor(by_parity(v[:]), products(acc), row2("L2_gnn_b3"), ALU.add).then_inc(s("silu_in"), 1)
            dve.wait_ge(s("node_mm"), 5 * M)
            link(V.tensor_tensor(by_parity(h[:]), by_parity(h[:]), products(acc), ALU.add))
            link(V.tensor_tensor(h[:], h[:], row("L2_gnn_b4"), ALU.add))
            normed(h[:])
            link(V.tensor_tensor(v[:], v[:], std[:].unsqueeze(2).broadcast_to([P, NT, D]), ALU.mult))
            link(V.tensor_tensor(v[:], v[:], row("L2_gnn_gamma"), ALU.mult))
            link(V.tensor_tensor(v[:], v[:], row("L2_gnn_beta"), ALU.add))
            link(V.tensor_tensor(xs[:], xs[:], v[:], ALU.add))
            pre_norm()
            dve.wait_ge(s("weights"), NW)
            V.tensor_reduce(rel_sum[:], wr3[:], AX, ALU.add).then_inc(s("rel_sum"), 1)
            dve.wait_ge(s("rel_ps"), 1)
            dve.wait_ge(s("rule_ps"), 1)
            V.tensor_copy(ruleT[:], aux[0:D, 512:512 + NR]).then_inc(s("rule_sb"), 1)
            link(V.tensor_scalar(rel_key[:], aux[:, 0:R3 * D].rearrange("p (r d) -> p r d", r=R3), 1.0 / D, None, ALU.mult))
            link(V.tensor_tensor(rel_key[:], rel_key[:], rows[:, ROWS.index("L3_gnn_Wk_bias"), :].unsqueeze(1).broadcast_to([P, R3, D]), ALU.add))
            dve.wait_ge(s("rule_ps"), 2)
            V.tensor_copy(key_rule[:], aux[:, 1024:1024 + NR]).then_inc(s("rule_sb"), 1)
            dve.wait_ge(s("node_mm"), 6 * M)
            link(V.tensor_tensor(by_parity(u[:]), products(acc), row2("L3_gnn_Wq_bias"), ALU.add))
            dve.sem_inc(s("u"), 1)
            three_parts(u[:], v[:], slice(0, D), "qn")
            dve.wait_ge(s("node_mm"), 7 * M)
            dve.wait_ge(s("qn"), 2)
            link(V.tensor_copy(by_parity(v[:, :, 0:NR]), products(acc, NR)))
            three_parts(v[:, :, 0:NR], v[:, :, 0:NR], slice(D, D + NR), "qn")
            tables(dve, 1, table_half)

            def before3(k, b):
                g = 2 * k + b
                dve.wait_ge(s("values"), g + 1)
                dve.wait_ge(s("scored"), g + 1)
                dve.wait_ge(s("used"), 3 * G + g + 1)
                stage_indices(idx3, g, b)
                build_onehots(3, g, b)

            def after3(k, b):
                g = 2 * k + b
                dve.wait_ge(s("qr_ps"), g + 1)
                dve.wait_ge(gat[b], 3 * (G // 2) * PER + (k + 1) * PER)
                for q in range(2):
                    qr = acc[:, (2 * b + q) * 512:(2 * b + q) * 512 + 4 * (D + NR)].rearrange("p (s d) -> p s d", s=4)
                    V.tensor_copy(rule_e[:, bass.ds(g * SG + 4 * q, 4), :], qr[:, :, D:D + NR])
                    V.tensor_tensor(msg[:, b, 4 * q:4 * q + 4, :], qr[:, :, 0:D], got[:, b, 4 * q:4 * q + 4, D:2 * D], ALU.mult).then_inc(s("prod"), 1)
                dve.wait_ge(s("prod"), 2 * (g + 1))
                V.tensor_reduce(base[:, bass.ds(g * SG, SG)], msg[:, b], AX, ALU.add).then_inc(s("scored"), 1)

            dve.sem_inc(s("scored"), 2)
            skewed(dve, before3, after3)
            flat3 = lambda t: t.rearrange("p c k -> p (c k)")
            L = SC * P
            BIG = 1e38

            def run_column(t, k):
                return t[:, :, k]

            link(V.tensor_scalar(keep_s[:], seg_start[:], -1.0, 1.0, ALU.mult, ALU.add))
            link(V.tensor_scalar(keep_e[:], seg_end[:], -1.0, 1.0, ALU.mult, ALU.add))
            for c in range(SC):
                V.tensor_tensor_scan(open_s[:, c, :], keep_s[:, c, :], zeros[:, 0:P], 1.0, ALU.mult, ALU.add)
                link(V.tensor_tensor_scan(open_e[:, c, ::-1], keep_e[:, c, ::-1], zeros[:, 0:P], 1.0, ALU.mult, ALU.add))
            link(V.tensor_copy(row_keep[:, 0], run_column(open_s, P - 1).unsqueeze(2).broadcast_to([P, SC, NR])))
            link(V.tensor_copy(row_keep[:, 1], run_column(open_e, 0).unsqueeze(2).broadcast_to([P, SC, NR])))
            link(V.memset(keep_s[:, :, 0:1], 0.0))
            link(V.memset(keep_e[:, :, P - 1:P], 0.0))
            dve.sem_inc(s("sm"), 1)
            dve.wait_ge(s("sm_ps"), 1)
            link(V.tensor_copy(carry_keep[:], aux[0:NR, 512:512 + 2 * L].rearrange("r (e i) -> r e i", e=2)))
            score = aux[:, 0:L]
            link(V.tensor_scalar(f1[:], valid[:], -1.0, BIG, ALU.add, ALU.mult))
            link(V.tensor_tensor(flat3(f2), score, flat3(valid), ALU.mult))
            link(V.tensor_tensor(f2[:], f2[:], f1[:], ALU.add))
            link(V.tensor_scalar(f1[:], keep_s[:], -1.0, BIG, ALU.add, ALU.mult))
            link(V.tensor_tensor_scan(flat3(f3), flat3(f1), flat3(f2), -BIG, ALU.add, ALU.max))
            V.tensor_copy(row_end[:, :, 0:1], f3[:, :, P - 1:P]).then_inc(s("sm"), 1)
            link(V.tensor_scalar(f1[:], open_s[:], -1.0, BIG, ALU.add, ALU.mult))
            link(V.tensor_scalar(carry_pen[:], carry_keep[0:1, 0, :], -1.0, BIG, ALU.add, ALU.mult))
            link(V.memset(carry[:], -BIG))
            dve.wait_ge(s("sm_ps"), 2)
            V.tensor_tensor_scan(carry[0:1, 1:L + 1], carry_pen[:], aux[0:1, 512:512 + L], -BIG, ALU.add, ALU.max).then_inc(s("sm"), 1)
            dve.wait_ge(s("sm_ps"), 3)
            link(V.tensor_copy(carry_col[:], aux[:, 1024:1024 + SC * NR].rearrange("p (c r) -> p c r", c=SC)))
            for c in range(SC):
                link(V.scalar_tensor_tensor(f3[:, c, :], f1[:, c, :], carry_col[:, c, 0:1], f3[:, c, :], ALU.add, ALU.max))

            steps = [3]

            def spread_back(forward, result, n):
                for r in range(n):
                    link(V.tensor_tensor(f1[:], forward(r), seg_end[:], ALU.mult))
                    link(V.tensor_tensor_scan(flat3(result(r))[:, ::-1], flat3(keep_e)[:, ::-1], flat3(f1)[:, ::-1], 0.0, ALU.mult, ALU.add))
                    link(V.tensor_copy(row_end[:, :, r:r + 1], result(r)[:, :, 0:1]))
                link(V.memset(carry[:], 0.0))
                dve.sem_inc(s("sm"), 1)
                dve.wait_ge(s("sm_ps"), steps[0] + 1)
                V.tensor_tensor_scan(carry[0:n, 0:L][:, ::-1], carry_keep[0:n, 1, ::-1], aux[0:n, 512:512 + L][:, ::-1], 0.0, ALU.mult, ALU.add).then_inc(s("sm"), 1)
                dve.wait_ge(s("sm_ps"), steps[0] + 2)
                steps[0] += 2
                link(V.tensor_copy(carry_col[:], aux[:, 1024:1024 + SC * NR].rearrange("p (c r) -> p c r", c=SC)))
                for r in range(n):
                    for c in range(SC):
                        link(V.scalar_tensor_tensor(result(r)[:, c, :], open_e[:, c, :], carry_col[:, c, r:r + 1], result(r)[:, c, :], ALU.mult, ALU.add))

            spread_back(lambda r: f3[:], lambda r: f2[:], 1)
            rules = acc.rearrange("p (r l) -> p r l", r=NR)
            pf = prob.rearrange("p r c k -> p r (c k)")
            qf = total.rearrange("p r c k -> p r (c k)")
            link(V.tensor_copy(flat3(f3), score))
            link(V.tensor_tensor(pf, rules, flat3(f3).unsqueeze(1).broadcast_to([P, NR, L]), ALU.add))
            link(V.tensor_tensor(qf, rules, flat3(f2).unsqueeze(1).broadcast_to([P, NR, L]), ALU.add))
            link(V.tensor_tensor(pf, pf, qf, ALU.subtract))
            V.tensor_scalar(pf, pf, 0.0, None, ALU.min).then_inc(s("exp_in"), 1)
            dve.wait_ge(s("exp_out"), 1)
            link(V.tensor_tensor(pf, pf, flat3(valid).unsqueeze(1).broadcast_to([P, NR, L]), ALU.mult))
            for r in range(NR):
                link(V.tensor_tensor_scan(qf[:, r, :], flat3(keep_s), pf[:, r, :], 0.0, ALU.mult, ALU.add))
                link(V.tensor_copy(row_end[:, :, r:r + 1], total[:, r, :, P - 1:P]))
            link(V.memset(carry[:], 0.0))
            dve.sem_inc(s("sm"), 1)
            dve.wait_ge(s("sm_ps"), steps[0] + 1)
            V.tensor_tensor_scan(carry[:, 1:L + 1], carry_keep[:, 0, :], aux[0:NR, 512:512 + L], 0.0, ALU.mult, ALU.add).then_inc(s("sm"), 1)
            dve.wait_ge(s("sm_ps"), steps[0] + 2)
            steps[0] += 2
            link(V.tensor_copy(carry_col[:], aux[:, 1024:1024 + SC * NR].rearrange("p (c r) -> p c r", c=SC)))
            for r in range(NR):
                for c in range(SC):
                    link(V.scalar_tensor_tensor(total[:, r, c, :], open_s[:, c, :], carry_col[:, c, r:r + 1], total[:, r, c, :], ALU.mult, ALU.add))
            spread_back(lambda r: total[:, r], lambda r: total[:, r], NR)
            link(V.tensor_scalar(qf, qf, 1e-30, None, ALU.max))
            link(V.reciprocal(qf, qf))
            link(V.tensor_tensor(pf, pf, qf, ALU.mult))
            link(V.tensor_reduce(flat3(f1), prob.rearrange("p r c k -> p (c k) r"), AX, ALU.add))
            V.tensor_scalar(f1[:], f1[:], 1.0 / NR, None, ALU.mult).then_inc(s("sm"), 1)
            dve.wait_ge(s("sm_ps"), steps[0] + 1)
            link(V.tensor_copy(base[:], aux[:, 0:L]))
            with dve.Fori(0, G // 2) as it:
                for b in range(2):
                    g = 2 * it + b
                    dve.wait_ge(s("used"), 4 * G + g + 1)
                    build_onehots(4, g, b)
                    V.tensor_tensor(msg[:, b], values[:, bass.ds(g * SG, SG), :],
                                    base[:, bass.ds(g * SG, SG)].unsqueeze(2).broadcast_to([P, SG, D]), ALU.mult).then_inc(s("weighed"), 1)
            dve.wait_ge(s("used"), 2 + 5 * G)
            link(V.tensor_tensor(h[:], tiles(acc), row("L3_gnn_bias"), ALU.add))
            normed(h[:])
            link(V.tensor_tensor(v[:], v[:], std[:].unsqueeze(2).broadcast_to([P, NT, D]), ALU.mult))
            link(V.tensor_tensor(v[:], v[:], row("L3_gnn_ln_g"), ALU.mult))
            link(V.tensor_tensor(v[:], v[:], row("L3_gnn_ln_b"), ALU.add))
            V.scalar_tensor_tensor(xs[:], v[:], 0.0, xs[:], ALU.max, ALU.add).then_inc(s("x_done"), 1)

        @block.scalar
        def _(act):
            A = nc.scalar
            roots, moved = [0], [0]
            act.sem_inc(s("ohT_sb"), 2)
            act.sem_inc(s("eaT_sb"), 1)
            act.sem_inc(s("values"), 2)

            def root():
                roots[0] += 1
                act.wait_ge(s("var"), roots[0])
                A.activation(std[:], var[:], ACT.Sqrt).then_inc(s("std"), 1)

            def take_transposed(dest):
                for m in range(0, M, 4):
                    n = min(4, M - m)
                    act.wait_ge(s("T_ps"), moved[0] + 1)
                    A.copy(dest[:, m:m + n, :], tp[moved[0] % 2][:, 0:n * P].rearrange("p (m k) -> p m k", m=n)).then_inc(s("T_sb"), 1)
                    moved[0] += 1

            def table_half(l, q, b, first=False):
                n = 4 * q + b
                act.wait_ge(s("tab_ps"), NT * l + n + 1)
                if not first:
                    act.wait_ge(tab[b], 16 * (l * len(range(b, NT, 4)) + q))
                if l == 0:
                    A.copy(stage[:, b, 512:1024], acc[:, (b % 2) * 1024 + 512:(b % 2) * 1024 + 1024]).then_inc(s("tabB"), 1)
                else:
                    A.copy(stage[:, b, :].rearrange("p (r q d) -> p r q d", q=2, d=D)[:, :, 0, :],
                           acc[:, (b % 2) * 1024:(b % 2) * 1024 + 512].rearrange("p (r d) -> p r d", d=D)).then_inc(s("tabB"), 1)

            def onehots_T(l, g, b):
                for q in range(2):
                    act.wait_ge(s("ohT_ps"), 2 * ((l - 2) * G + g) + q + 1)
                    A.copy(ohT[:, b, 4 * q:4 * q + 4, :], tp[q].bitcast(bf16)[:, 0:4 * P].rearrange("p (s k) -> p s k", s=4)).then_inc(s("ohT_sb"), 1)

            root()
            take_transposed(hT)
            tables(act, 0, table_half)
            root()
            take_transposed(hT)
            take_transposed(uT)
            act.wait_ge(s("elu_in"), 1)
            A.activation(v[:], v[:], ACT.Exp).then_inc(s("elu_exp"), 1)
            root()
            take_transposed(hT)

            def before2(k, b):
                g = 2 * k + b
                onehots_T(2, g, b)
                act.wait_ge(s("eaT_ps"), g + 3)
                A.copy(eaT[:, b], tp[0][:, 0:2 * P].rearrange("p (q k) -> p q k", q=2)).then_inc(s("eaT_sb"), 1)

            def after2(k, b):
                g = 2 * k + b
                act.wait_ge(s("edge_sum"), g + 1)
                A.activation(msg[:, b], got1[b], ACT.Silu).then_inc(s("silu"), 1)

            skewed(act, before2, after2)
            take_transposed(uT)
            take_transposed(uT)
            act.wait_ge(s("silu_in"), 1)
            A.activation(u[:], v[:], ACT.Silu).then_inc(s("u"), 1)
            take_transposed(uT)
            root()
            root()
            take_transposed(hT)
            take_transposed(uT)
            tables(act, 1, table_half)

            def before3(k, b):
                onehots_T(3, 2 * k + b, b)

            def after3(k, b):
                g = 2 * k + b
                act.wait_ge(gat[b], 3 * (G // 2) * PER + (k + 1) * PER)
                A.copy(values[:, bass.ds(g * SG, SG), :], got[:, b, :, 0:D]).then_inc(s("values"), 1)

            skewed(act, before3, after3)
            act.wait_ge(s("exp_in"), 1)
            A.activation(prob, prob, ACT.Exp, scale=float(D) ** -0.5).then_inc(s("exp_out"), 1)
            root()

        @block.tensor
        def _(pe):
            T = nc.tensor
            moved, mms = [0], [0]
            pe.sem_inc(s("used"), 2)
            pe.sem_inc(s("eaT_ps"), 2)

            pe.wait_ge(s("const"), 3)
            pe.wait_ge(s("reach"), 1)
            for c in range(SC):
                last = T.matmul(aux[:, c * P:(c + 1) * P], reach[:, c:c + 1].broadcast_to([P, P]), ident[:], start=True, stop=True)
            last.then_inc(s("reach_row"), 1)
            pe.wait_ge(s("slot_t"), 1)
            for c in range(SC):
                last = T.transpose(aux[0:1, 512 + c * P:512 + (c + 1) * P], slot_n[:, c:c + 1], ident[:])
            last.then_inc(s("rows_ps"), 1)
            pe.wait_ge(s("work"), 1)
            for j in range(4):
                for c in range(SC):
                    last = T.transpose(aux[:, 512 * j + c * P:512 * j + (c + 1) * P], work[j][:, c, :], ident[:])
                last.then_inc(s("work_T"), 1)
            pe.wait_ge(s("tables_made"), 1)
            pe.wait_ge(s("weights"), NW)
            for q, (rows_, wT) in enumerate(((wl_rows, wlT), (wr_rows, wrT))):
                T.transpose(aux[:, q * D:(q + 1) * D], rows_[:].rearrange("o q i -> o (q i)"), ident[0:D, 0:D]).then_inc(s("wT_ps"), 1)

            def node_transposes(src, signal, count):
                pe.wait_ge(s(signal), count)
                for m in range(0, M, 4):
                    if moved[0] >= 2:
                        pe.wait_ge(s("T_sb"), moved[0] - 1)
                    for j in range(m, min(M, m + 4)):
                        last = T.transpose(tp[moved[0] % 2][:, (j - m) * P:(j - m + 1) * P], src[:, 2 * j:2 * j + 2, :].rearrange("p t d -> p (t d)"), ident[:])
                    last.then_inc(s("T_ps"), 1)
                    moved[0] += 1
                pe.wait_ge(s("T_sb"), moved[0])

            def node_products(*outs):
                for m in range(M):
                    for q in range(2):
                        hf = slice(q * D, (q + 1) * D)
                        for dest, w, terms in outs:
                            for j, (lhs, rhs) in enumerate(terms):
                                last = T.matmul(dest[:, q * 1024 + m * w:q * 1024 + (m + 1) * w], lhs[hf, m, :], rhs[hf],
                                                start=(j == 0), stop=(j == len(terms) - 1), skip_group_check=True)
                    last.then_inc(s("node_mm"), 1)

            def table_ps(l, n):
                hf = slice((n % 2) * D, (n % 2) * D + D)
                lhs = hT[hf, n // 2, :]
                if l or n >= 2:
                    pe.wait_ge(s("tabA"), NT * l + n - 1)
                    pe.wait_ge(s("tabB"), NT * l + n - 1)
                at_ = (n % 2) * 1024
                if l == 0:
                    for r in range(2):
                        last = T.matmul(acc[:, at_ + 512 * r:at_ + 512 * r + 512], lhs, w0[hf].rearrange("p r d -> p (r d)")[:, 512 * r:512 * r + 512], start=True, stop=True)
                else:
                    T.matmul(acc[:, at_:at_ + 512], lhs, wr3[hf].rearrange("p r d -> p (r d)"), start=True, stop=True)
                    last = T.matmul(acc[:, at_ + 512:at_ + 512 + D], lhs, wk1[hf], start=True, stop=True)
                last.then_inc(s("tab_ps"), 1)

            def clear_sums():
                for c in range(4):
                    T.matmul(acc[:, 512 * c:512 * c + 512], zeros[:, 0:P], zeros[:], start=True, stop=True, skip_group_check=True)

            def sum_into_nodes(b, n, rows_, counts=False):
                for j in range(SG):
                    last = T.matmul(acc[:, bass.ds(n[j] * D, D)], oh[:, b, j, :], rows_[:, j, :], start=False, stop=True, skip_group_check=True)
                    if counts:
                        last = T.matmul(acc[:, bass.ds(n[j] + C, 1)], oh[:, b, j, :], ones[:], start=False, stop=True, skip_group_check=True)
                last.then_inc(s("used"), 1)

            def gathered_sums(l):
                with pe.Fori(0, G // 2) as it:
                    for b in range(2):
                        g = 2 * it + b
                        n = slot_tiles(PE_, g)
                        pe.wait_ge(s("oh"), l * G + g + 1)
                        pe.wait_ge(gat[b], l * (G // 2) * PER + (it + 1) * PER)
                        sum_into_nodes(b, n, got1[b], counts=(l == 0))

            def onehots_T(l, g, b):
                pe.wait_ge(s("oh"), l * G + g + 1)
                if l == 2:
                    pe.wait_ge(s("eaT_sb"), g + 1)
                for q in range(2):
                    pe.wait_ge(s("ohT_sb"), 2 * ((l - 2) * G + g) + q + 1)
                    for j in range(4):
                        last = T.transpose(tp[q].bitcast(bf16)[:, j * P:(j + 1) * P], ohb[:, b, 4 * q + j, :], ident_h[:])
                    last.then_inc(s("ohT_ps"), 1)

            pe.wait_ge(s("wT_sb"), 1)
            node_transposes(h, "h", 1)
            for n in range(NT):
                table_ps(0, n)
            pe.wait_ge(s("tabA"), NT)
            pe.wait_ge(s("tabB"), NT)
            pe.wait_ge(s("n_row"), 1)
            clear_sums()
            gathered_sums(0)
            node_transposes(h, "h", 2)
            clear_sums()
            gathered_sums(1)
            node_transposes(u, "u", 1)
            node_products((acc, D, [(uT, wlT), (hT, wrT)]))
            node_transposes(h, "h", 3)
            node_products((acc, D, [(hT, w1ab[:, 0, :])]), (aux, D, [(hT, w1ab[:, 1, :])]))
            pe.wait_ge(s("plain_table"), 2)
            pe.wait_ge(s("qn"), 1)
            clear_sums()

            def before2(k, b):
                g = 2 * k + b
                onehots_T(2, g, b)
                pe.wait_ge(eas[b], (k + 1) * PER)
                pe.wait_ge(s("ohT_sb"), 2 * g + 3)
                for q in range(2):
                    last = T.transpose(tp[0][:, q * P:(q + 1) * P], ea[:, b, q * P:(q + 1) * P], ident[:])
                last.then_inc(s("eaT_ps"), 1)

            def scatter2(k, b):
                g = 2 * k + b
                n = slot_tiles(PE_, g)
                pe.wait_ge(s("silu"), g + 1)
                sum_into_nodes(b, n, msg[:, b])

            def edges2(k, b):
                g = 2 * k + b
                n = slot_tiles(PE_, g)
                pe.wait_ge(s("ohT_sb"), 2 * (g + 1) + 2)
                pe.wait_ge(s("eaT_sb"), g + 2)
                for q in range(2):
                    T.matmul(eb[b][:, 256 * q:256 * q + 256], eaT[:, b, q, :], w1c.rearrange("p s d -> p (s d)"), start=True, stop=False, skip_group_check=True)
                    for j in range(4 * q, 4 * q + 4):
                        for part in range(3):
                            last = T.matmul(eb[b][:, j * D:(j + 1) * D], ohT[:, b, j, :], qn[:, part, bass.ds(n[j], 1), 0:D].rearrange("p t d -> p (t d)"), start=False, stop=True, skip_group_check=True)
                last.then_inc(s("eb_ps"), 1)

            before2(0, 0)
            edges2(0, 0)
            with pe.Fori(0, G // 2 - 1) as it:
                before2(it, 1)
                scatter2(it, 0)
                edges2(it, 1)
                before2(it + 1, 0)
                scatter2(it, 1)
                edges2(it + 1, 0)
            before2(G // 2 - 1, 1)
            scatter2(G // 2 - 1, 0)
            edges2(G // 2 - 1, 1)
            scatter2(G // 2 - 1, 1)

            node_transposes(u, "u", 2)
            node_products((acc, D, [(uT, w2)]))
            node_transposes(u, "u", 3)
            node_products((acc, D, [(hT, w3[:, 0, :]), (uT, w3[:, 1, :])]))
            node_transposes(u, "u", 4)
            node_products((acc, D, [(uT, w4)]))
            node_transposes(h, "h", 4)
            pe.wait_ge(s("rel_sum"), 1)
            for r in range(R3):
                last = T.matmul(aux[:, r * D:(r + 1) * D], rel_sum[0:D, r:r + 1].broadcast_to([D, P]), wk2[:], start=True, stop=True)
            last.then_inc(s("rel_ps"), 1)
            pe.wait_ge(s("rule_rows"), 16)
            T.matmul(aux[0:D, 512:512 + NR], rule_rows[:], ident[0:NR, 0:NR], start=True, stop=True).then_inc(s("rule_ps"), 1)
            pe.wait_ge(s("rule_sb"), 1)
            T.matmul(aux[:, 1024:1024 + NR], wk3[:].rearrange("p q d -> p (q d)"), ruleT[:], start=True, stop=True).then_inc(s("rule_ps"), 1)
            node_products((acc, D, [(hT, wq)]))
            pe.wait_ge(s("rule_sb"), 2)
            node_transposes(u, "u", 5)
            node_products((acc, NR, [(uT, key_rule)]))
            pe.wait_ge(s("qn"), 3)
            for n in range(NT):
                table_ps(1, n)
            pe.wait_ge(s("tabA"), 2 * NT)
            pe.wait_ge(s("tabB"), 2 * NT)

            with pe.Fori(0, G // 2) as it:
                for b in range(2):
                    g = 2 * it + b
                    onehots_T(3, g, b)
                    n = slot_tiles(PE_, g)
                    pe.wait_ge(s("scored"), g + 1)
                    pe.wait_ge(s("values"), g + 1)
                    for q in range(2):
                        pe.wait_ge(s("ohT_sb"), 2 * (G + g) + q + 3)
                        for j in range(4):
                            at_ = (2 * b + q) * 512 + j * (D + NR)
                            for part in range(3):
                                last = T.matmul(acc[:, at_:at_ + D + NR], ohT[:, b, 4 * q + j, :], qn[:, part, bass.ds(n[4 * q + j], 1), :].rearrange("p t d -> p (t d)"),
                                                start=(part == 0), stop=(part == 2))
                    last.then_inc(s("qr_ps"), 1)
                    pe.sem_inc(s("used"), 1)

            pe.wait_ge(s("sm"), 1)
            pe.wait_ge(s("values"), 2 + G)
            for c in range(SC):
                T.transpose(aux[:, c * P:(c + 1) * P], base[:, c * P:(c + 1) * P], ident[:])
                for r in range(NR):
                    T.transpose(acc[:, r * SC * P + c * P:r * SC * P + (c + 1) * P], rule_e[:, c * P:(c + 1) * P, r], ident[:])
                for e in range(2):
                    at_ = 512 + e * SC * P + c * P
                    last = T.transpose(aux[0:NR, at_:at_ + P], row_keep[:, e, c, :], ident[:])
            last.then_inc(s("sm_ps"), 1)
            for j, n in enumerate((1, 1, NR, NR)):
                pe.wait_ge(s("sm"), 2 * j + 2)
                for c in range(SC):
                    last = T.transpose(aux[0:n, 512 + c * P:512 + (c + 1) * P], row_end[:, c, 0:n], ident[:])
                last.then_inc(s("sm_ps"), 1)
                pe.wait_ge(s("sm"), 2 * j + 3)
                for c in range(SC):
                    at_ = c * P + j % 2
                    last = T.matmul(aux[:, 1024 + c * NR:1024 + (c + 1) * NR], carry[:, at_:at_ + P], ident[0:NR, 0:NR], start=True, stop=True)
                last.then_inc(s("sm_ps"), 1)
            pe.wait_ge(s("sm"), 10)
            for c in range(SC):
                last = T.transpose(aux[:, c * P:(c + 1) * P], f1[:, c, :], ident[:])
            last.then_inc(s("sm_ps"), 1)
            clear_sums()
            with pe.Fori(0, G // 2) as it:
                for b in range(2):
                    g = 2 * it + b
                    n = slot_tiles(PE_, g)
                    pe.wait_ge(s("oh"), 4 * G + g + 1)
                    pe.wait_ge(s("weighed"), g + 1)
                    sum_into_nodes(b, n, msg[:, b])


INS = ["x", "src", "dst", "edge_attr_32", "edge_type_16", "edge_type_8", "L0_gnn_weight", "L1_gnn_W_l", "L1_gnn_b_l", "L1_gnn_W_r",
       "L2_gnn_w1", "L2_gnn_b1", "L2_gnn_w2", "L2_gnn_b2", "L2_gnn_w3", "L2_gnn_b3", "L2_gnn_w4", "L2_gnn_b4", "L2_gnn_gamma", "L2_gnn_beta",
       "L3_gnn_rule_ids", "L3_gnn_W_r", "L3_gnn_Wq_w", "L3_gnn_Wq_bias", "L3_gnn_Wk_w", "L3_gnn_Wk_bias", "L3_gnn_rule_emb", "L3_gnn_bias",
       "L3_gnn_ln_g", "L3_gnn_ln_b"]


def kernel(**inputs):
    import numpy as np
    import concourse.bacc as bacc
    from concourse.bass_utils import run_bass_kernel_spmd as run

    nc = bacc.Bacc("TRN2", target_bir_lowering=False, num_devices=1)
    arrays = {name: np.ascontiguousarray(inputs[name]) for name in INS}
    a = {name: nc.dram_tensor(name, v.shape, mybir.dt.from_np(v.dtype), kind="ExternalInput").ap() for name, v in arrays.items()}
    N, E = arrays["x"].shape[0], arrays["src"].shape[0]
    out = nc.dram_tensor("out", arrays["x"].shape, mybir.dt.float32, kind="ExternalOutput").ap()
    network(nc, a, out, N, E)
    return run(nc, [arrays], core_ids=[0]).results[0]["out"]
```
